# Optimizing a Trainium2 kernel written in Bass

```python
import numpy as np
import jax
import jax.numpy as jnp

def _softmax(x, axis=-1):
    return jax.nn.softmax(x, axis=axis)

def _gelu(x):
    return jax.nn.gelu(x, approximate=True)

def _silu(x):
    return jax.nn.silu(x)

def _sigmoid(x):
    return jax.nn.sigmoid(x)

def _layernorm(x, axis=-1, eps=1e-05):
    m = jnp.mean(x, axis=axis, keepdims=True)
    v = jnp.var(x, axis=axis, keepdims=True)
    return (x - m) / jnp.sqrt(v + eps)

def _scatter_add(tgt, idx, src, axis=0):
    return tgt.at[idx].add(src)

def _segment_sum(src, seg, n):
    return jax.ops.segment_sum(src, seg, n)
kernel_name = 'mk_adaln_d2_jaxref_r8_c59dfc'

def setup_inputs(seed: int=0):
    np.random.seed(seed)
    _w = jnp.asarray

    def _L0_attn_setup():
        import jax, jax.numpy as jnp
        import numpy as np
        B, S, H, NH, MRP = (4, 128, 128, 16, 64)
        DK = H // NH
        VOCAB = 2 * MRP + 1

        def _rel_idx(seq_len):
            r = jnp.arange(seq_len)
            dist = r[None, :] - r[:, None]
            return jnp.clip(dist, -MRP, MRP) + MRP
        key = jax.random.key(seed)
        ks = jax.random.split(key, 12)
        sc = 1.0 / np.sqrt(H)
        inp = {'x': jax.random.normal(ks[0], (B, S, H), jnp.float32), 'mask': jnp.ones((B, S), jnp.int32), 'Wq': jax.random.normal(ks[1], (H, H), jnp.float32) * sc, 'bq': jnp.zeros((H,), jnp.float32), 'Wk': jax.random.normal(ks[2], (H, H), jnp.float32) * sc, 'bk': jnp.zeros((H,), jnp.float32), 'Wv': jax.random.normal(ks[3], (H, H), jnp.float32) * sc, 'bv': jnp.zeros((H,), jnp.float32), 'Wo': jax.random.normal(ks[4], (H, H), jnp.float32) * sc, 'bo': jnp.zeros((H,), jnp.float32), 'embK': jax.random.normal(ks[5], (VOCAB, DK), jnp.float32), 'embV': jax.random.normal(ks[6], (VOCAB, DK), jnp.float32)}
        return inp
    _L0_attn_in = _L0_attn_setup()

    def _L0_ffn_setup():
        import math
        import jax, jax.numpy as jnp
        import numpy as np
        D_MODEL = 128
        D_FF = 512
        E = 8
        K = 2
        CF = 1.25
        CLAMP = 10000.0
        key = jax.random.key(seed)
        k0, k1, k2, k3 = jax.random.split(key, 4)
        B, S = (4, 256)
        x = jax.random.normal(k0, (B, S, D_MODEL), dtype=jnp.float32)
        ln_gamma = jnp.ones((D_MODEL,), jnp.float32)
        ln_beta = jnp.zeros((D_MODEL,), jnp.float32)
        rb = 0.02 * math.sqrt(3.0)
        Wr = jax.random.uniform(k1, (E, D_MODEL), jnp.float32, -rb, rb)
        b12 = math.sqrt(6.0 / (D_MODEL + 2 * D_FF))
        W12 = jax.random.uniform(k2, (E, 2 * D_FF, D_MODEL), jnp.float32, -b12, b12)
        b3 = math.sqrt(6.0 / (D_FF + D_MODEL))
        W3 = jax.random.uniform(k3, (E, D_MODEL, D_FF), jnp.float32, -b3, b3)
        return {'x': x, 'ln_gamma': ln_gamma, 'ln_beta': ln_beta, 'Wr': Wr, 'W12': W12, 'W3': W3}
    _L0_ffn_in = _L0_ffn_setup()
    _L0_c = _w((lambda *s: np.random.randn(*s).astype(np.float32) * 0.05)(8, 128))
    _L0_wmod = _w((lambda *s: np.random.randn(*s).astype(np.float32) * 0.05)(128, 6 * 128) * 128 ** (-0.5))

    def _L1_attn_setup():
        import jax, jax.numpy as jnp
        import numpy as np
        import math
        DIM = 128
        HEADS = 16
        HEAD_DIM = DIM // HEADS
        B, N = (1, 512)
        key = jax.random.key(seed)
        k1, k2, k3, k4 = jax.random.split(key, 4)
        content = jax.random.normal(k1, (B, N, DIM), dtype=jnp.float32)
        Wq = jnp.eye(DIM, dtype=jnp.float32) + 0.02 * jax.random.normal(k2, (DIM, DIM), dtype=jnp.float32)
        Wk = jnp.eye(DIM, dtype=jnp.float32) + 0.02 * jax.random.normal(k3, (DIM, DIM), dtype=jnp.float32)
        Wv = jnp.eye(DIM, dtype=jnp.float32) + 0.02 * jax.random.normal(k4, (DIM, DIM), dtype=jnp.float32)
        return {'content': content, 'Wq': Wq, 'Wk': Wk, 'Wv': Wv}
    _L1_attn_in = _L1_attn_setup()

    def _L1_ffn_setup():
        import jax, jax.numpy as jnp
        import numpy as np
        BLOCK = 16
        _GRID = jnp.array([0.0, 0.5, 1.0, 1.5, 2.0, 3.0, 4.0, 6.0], dtype=jnp.float32)
        _MID = jnp.array([0.25, 0.75, 1.25, 1.75, 2.5, 3.5, 5.0], dtype=jnp.float32)

        def fp4_quant_dequant(x):
            shape = x.shape
            xb = x.reshape(shape[:-1] + (shape[-1] // BLOCK, BLOCK))
            scale = jnp.max(jnp.abs(xb), axis=-1, keepdims=True) / 6.0
            scale = jnp.maximum(scale, jnp.float32(1e-12))
            xn = xb / scale
            idx = jnp.searchsorted(_MID, jnp.abs(xn))
            q = _GRID[idx] * jnp.sign(xn) * scale
            return q.reshape(shape)

        def fp4_linear(x, w):
            xq = fp4_quant_dequant(x)
            wq = fp4_quant_dequant(w)
            return jnp.einsum('bsk,nk->bsn', xq, wq)
        key = jax.random.key(seed)
        k1, k2, k3, k4 = jax.random.split(key, 4)
        H, I = (128, 352)
        x = jax.random.normal(k1, (4, 512, H), dtype=jnp.float32)
        w_gate = jax.random.normal(k2, (I, H), dtype=jnp.float32) * 0.02
        w_up = jax.random.normal(k3, (I, H), dtype=jnp.float32) * 0.02
        w_down = jax.random.normal(k4, (H, I), dtype=jnp.float32) * 0.02
        return {'x': x, 'w_gate': w_gate, 'w_up': w_up, 'w_down': w_down}
    _L1_ffn_in = _L1_ffn_setup()
    _L1_c = _w((lambda *s: np.random.randn(*s).astype(np.float32) * 0.05)(8, 128))
    _L1_wmod = _w((lambda *s: np.random.randn(*s).astype(np.float32) * 0.05)(128, 6 * 128) * 128 ** (-0.5))
    _d = {'L0_attn_x': _L0_attn_in['x'], 'L0_attn_mask': _L0_attn_in['mask'], 'L0_attn_Wq': _L0_attn_in['Wq'], 'L0_attn_bq': _L0_attn_in['bq'], 'L0_attn_Wk': _L0_attn_in['Wk'], 'L0_attn_bk': _L0_attn_in['bk'], 'L0_attn_Wv': _L0_attn_in['Wv'], 'L0_attn_bv': _L0_attn_in['bv'], 'L0_attn_Wo': _L0_attn_in['Wo'], 'L0_attn_bo': _L0_attn_in['bo'], 'L0_attn_embK': _L0_attn_in['embK'], 'L0_attn_embV': _L0_attn_in['embV'], 'L0_ffn_ln_gamma': _L0_ffn_in['ln_gamma'], 'L0_ffn_ln_beta': _L0_ffn_in['ln_beta'], 'L0_ffn_Wr': _L0_ffn_in['Wr'], 'L0_ffn_W12': _L0_ffn_in['W12'], 'L0_ffn_W3': _L0_ffn_in['W3'], 'L0_c': _L0_c, 'L0_wmod': _L0_wmod, 'L1_attn_Wq': _L1_attn_in['Wq'], 'L1_attn_Wk': _L1_attn_in['Wk'], 'L1_attn_Wv': _L1_attn_in['Wv'], 'L1_ffn_w_gate': _L1_ffn_in['w_gate'], 'L1_ffn_w_up': _L1_ffn_in['w_up'], 'L1_ffn_w_down': _L1_ffn_in['w_down'], 'L1_c': _L1_c, 'L1_wmod': _L1_wmod}
    _x0 = _d['L0_attn_x']
    _d['L0_attn_x'] = jax.random.normal(jax.random.fold_in(jax.random.key(seed), 1), (8, 256, 128), dtype=_x0.dtype)
    del _x0
    return _d

def reference(L0_attn_x, L0_attn_mask, L0_attn_Wq, L0_attn_bq, L0_attn_Wk, L0_attn_bk, L0_attn_Wv, L0_attn_bv, L0_attn_Wo, L0_attn_bo, L0_attn_embK, L0_attn_embV, L0_ffn_ln_gamma, L0_ffn_ln_beta, L0_ffn_Wr, L0_ffn_W12, L0_ffn_W3, L0_c, L0_wmod, L1_attn_Wq, L1_attn_Wk, L1_attn_Wv, L1_ffn_w_gate, L1_ffn_w_up, L1_ffn_w_down, L1_c, L1_wmod):

    def _L0_attn_ref(x, mask, Wq, bq, Wk, bk, Wv, bv, Wo, bo, embK, embV):
        import jax, jax.numpy as jnp
        import numpy as np
        B, S, H, NH, MRP = (4, 128, 128, 16, 64)
        DK = H // NH
        VOCAB = 2 * MRP + 1

        def _rel_idx(seq_len):
            r = jnp.arange(seq_len)
            dist = r[None, :] - r[:, None]
            return jnp.clip(dist, -MRP, MRP) + MRP
        nb, seq_len, _ = x.shape
        idx = _rel_idx(seq_len)
        rk = embK[idx]
        rv = embV[idx]

        def proj(W, b):
            return (x @ W.T + b).reshape(nb, seq_len, NH, DK).transpose(0, 2, 1, 3)
        q = proj(Wq, bq)
        k = proj(Wk, bk)
        v = proj(Wv, bv)
        logits = jnp.einsum('bhqd,bhkd->bhqk', q, k) + jnp.einsum('bhqd,qkd->bhqk', q, rk)
        w = jax.nn.softmax(logits, axis=-1)
        out = jnp.einsum('bhqk,bhkd->bhqd', w, v) + jnp.einsum('bhqk,qkd->bhqd', w, rv)
        out = out.transpose(0, 2, 1, 3).reshape(nb, seq_len, NH * DK)
        return out @ Wo.T + bo

    def _L0_ffn_ref(x, ln_gamma, ln_beta, Wr, W12, W3):
        import math
        import jax, jax.numpy as jnp
        import numpy as np
        D_MODEL = 128
        D_FF = 512
        E = 8
        K = 2
        CF = 1.25
        CLAMP = 10000.0
        B, S, D = x.shape
        T = B * S
        xf = x.reshape(T, D)
        mu = xf.mean(-1, keepdims=True)
        var = ((xf - mu) ** 2).mean(-1, keepdims=True)
        xn = (xf - mu) / jnp.sqrt(var + 1e-05) * ln_gamma + ln_beta
        logits = jnp.clip(xn @ Wr.T, -CLAMP, CLAMP)
        m = logits.max(-1, keepdims=True)
        ex = jnp.exp(logits - m)
        probs = ex / (ex.sum(-1, keepdims=True) + 1e-12)
        top_p, top_i = jax.lax.top_k(probs, K)
        Sslots = T * K
        experts = top_i.reshape(-1)
        weights = top_p.reshape(-1)
        tokens = jnp.repeat(jnp.arange(T, dtype=jnp.int32), K)
        order = jnp.argsort(experts, stable=True)
        e_s = experts[order]
        w_s = weights[order]
        t_s = tokens[order]
        counts = jnp.bincount(e_s, length=E)
        offsets = jnp.concatenate([jnp.zeros((1,), counts.dtype), jnp.cumsum(counts)])
        rank = jnp.arange(Sslots, dtype=counts.dtype) - offsets[e_s]
        cap = max(1, math.ceil(math.ceil(T * K * CF) / E))
        kept = rank < cap
        pos = jnp.where(kept, rank, cap)
        buf = jnp.zeros((E, cap, D), x.dtype).at[e_s, pos].set(xn[t_s], mode='drop')
        gu = jnp.einsum('ecd,efd->ecf', buf, W12)
        g, u = (gu[..., :D_FF], gu[..., D_FF:])
        h = jax.nn.silu(g) * u
        y = jnp.einsum('ecf,edf->ecd', h, W3)
        y_slot = y[e_s, jnp.minimum(pos, cap - 1)] * (w_s * kept.astype(x.dtype))[:, None]
        out = jnp.zeros((T, D), x.dtype).at[t_s].add(y_slot)
        return out.reshape(B, S, D)

    def _L1_attn_ref(content, Wq, Wk, Wv):
        import jax, jax.numpy as jnp
        import numpy as np
        import math
        DIM = 128
        HEADS = 16
        HEAD_DIM = DIM // HEADS
        B, N = (1, 512)
        b, n, d = content.shape
        Q = (content @ Wq).reshape(b, n, HEADS, HEAD_DIM)
        K = (content @ Wk).reshape(b, n, HEADS, HEAD_DIM)
        V = (content @ Wv).reshape(b, n, HEADS, HEAD_DIM)
        scores = jnp.einsum('bqhd,bkhd->bhqk', Q, K) / math.sqrt(HEAD_DIM)
        alpha = jax.nn.softmax(scores, axis=-1)
        causal = jnp.tril(jnp.ones((n, n), dtype=bool))
        alpha = jnp.where(causal, alpha, jnp.zeros((), dtype=alpha.dtype))
        Y = jnp.einsum('bhqk,bkhd->bqhd', alpha, V).reshape(b, n, d)
        return Y

    def _L1_ffn_ref(x, w_gate, w_up, w_down):
        import jax, jax.numpy as jnp
        import numpy as np
        BLOCK = 16
        _GRID = jnp.array([0.0, 0.5, 1.0, 1.5, 2.0, 3.0, 4.0, 6.0], dtype=jnp.float32)
        _MID = jnp.array([0.25, 0.75, 1.25, 1.75, 2.5, 3.5, 5.0], dtype=jnp.float32)

        def fp4_quant_dequant(x):
            shape = x.shape
            xb = x.reshape(shape[:-1] + (shape[-1] // BLOCK, BLOCK))
            scale = jnp.max(jnp.abs(xb), axis=-1, keepdims=True) / 6.0
            scale = jnp.maximum(scale, jnp.float32(1e-12))
            xn = xb / scale
            idx = jnp.searchsorted(_MID, jnp.abs(xn))
            q = _GRID[idx] * jnp.sign(xn) * scale
            return q.reshape(shape)

        def fp4_linear(x, w):
            xq = fp4_quant_dequant(x)
            wq = fp4_quant_dequant(w)
            return jnp.einsum('bsk,nk->bsn', xq, wq)
        gate = fp4_linear(x, w_gate)
        y = fp4_linear(x, w_up)
        h = jax.nn.silu(gate) * y
        return fp4_linear(h, w_down)
    x = L0_attn_x
    mod = (_silu(L0_c) @ L0_wmod).reshape(L0_c.shape[0], 6, 1, -1)
    sa, ca, ga, sb, cb, gb = (mod[:, 0], mod[:, 1], mod[:, 2], mod[:, 3], mod[:, 4], mod[:, 5])
    ga = (2 * (ga >= 0) - 1) * jnp.maximum(jnp.abs(ga), 0.25)
    gb = (2 * (gb >= 0) - 1) * jnp.maximum(jnp.abs(gb), 0.25)
    h = _layernorm(x, axis=-1) * (1 + ca) + sa
    x = x + ga * _L0_attn_ref(h, L0_attn_mask, L0_attn_Wq, L0_attn_bq, L0_attn_Wk, L0_attn_bk, L0_attn_Wv, L0_attn_bv, L0_attn_Wo, L0_attn_bo, L0_attn_embK, L0_attn_embV)
    h = _layernorm(x, axis=-1) * (1 + cb) + sb
    x = x + gb * _L0_ffn_ref(h, L0_ffn_ln_gamma, L0_ffn_ln_beta, L0_ffn_Wr, L0_ffn_W12, L0_ffn_W3)
    mod = (_silu(L1_c) @ L1_wmod).reshape(L1_c.shape[0], 6, 1, -1)
    sa, ca, ga, sb, cb, gb = (mod[:, 0], mod[:, 1], mod[:, 2], mod[:, 3], mod[:, 4], mod[:, 5])
    ga = (2 * (ga >= 0) - 1) * jnp.maximum(jnp.abs(ga), 0.25)
    gb = (2 * (gb >= 0) - 1) * jnp.maximum(jnp.abs(gb), 0.25)
    h = _layernorm(x, axis=-1) * (1 + ca) + sa
    x = x + ga * _L1_attn_ref(h, L1_attn_Wq, L1_attn_Wk, L1_attn_Wv)
    h = _layernorm(x, axis=-1) * (1 + cb) + sb
    x = x + gb * _L1_ffn_ref(h, L1_ffn_w_gate, L1_ffn_w_up, L1_ffn_w_down)
    return x

_drawn_inputs = setup_inputs


def setup_inputs(seed=0):
    import zlib

    import numpy as np

    out = dict(_drawn_inputs(seed))
    spreads = {'L0_attn_bq': (0.0, 0.1),
     'L0_attn_bk': (0.0, 2.0),
     'L0_attn_bv': (0.0, 0.345),
     'L0_attn_bo': (0.0, 0.324),
     'L0_ffn_ln_gamma': (1.0, 0.6),
     'L0_ffn_ln_beta': (0.0, 0.8)}
    factors = {'L0_ffn_Wr': 7.006,
     'L0_ffn_W12': 6.091,
     'L0_ffn_W3': 6.103,
     'L1_ffn_w_gate': 8.0,
     'L1_ffn_w_up': 8.0,
     'L1_ffn_w_down': 8.0,
     'L1_attn_Wq': 7.464,
     'L1_attn_Wk': 8.0,
     'L1_attn_Wv': 7.445}
    for name, (base, spread) in spreads.items():
        noise = np.random.default_rng([zlib.crc32(name.encode()), seed]).standard_normal(out[name].shape)
        drawn = base * np.exp(spread * noise) if base else spread * noise
        out[name] = jnp.asarray(drawn.astype(out[name].dtype))
    for name, factor in factors.items():
        out[name] = (out[name] * factor).astype(out[name].dtype)
    return out
```

```python
from contextlib import ExitStack

import concourse.bass as bass
from concourse import mybir

F32 = mybir.dt.float32
BF16 = mybir.dt.bfloat16
I32 = mybir.dt.int32
U32 = mybir.dt.uint32
ALU = mybir.AluOpType
ACT = mybir.ActivationFunctionType
AX = mybir.AxisListType

P = 128
B, S = 8, 256
NT = B * S // P
TB = S // P
NH, DH = 16, 8
HG = NH // 2
QB = P // HG
NJ = S // QB
MRP = 64
UNITS = 16
EPS = 1e-5
E, FF = 8, 512
CAP = 640
ET = CAP // P
SLOTS = E * CAP
FC = FF // P
FI = 352
QBLK = 16
GA0, CB0, SB0, GB0, GA1, CB1, SB1, GB1 = range(8)


class Chain:

    def __init__(self, eng, sem, per=0, turn=0):
        self.eng, self.sem, self.per, self.at, self.turn = eng, sem, per, 0, turn

    def step(self, ins):
        self.at += 1
        ins.then_inc(self.sem, 1)

    def join(self):
        self.eng.wait_ge(self.sem, self.turn * self.per + self.at)

    def link(self, ins):
        self.step(ins)
        self.join()

    def end(self):
        assert self.at == self.per, (self.at, self.per)


def every_batch(eng, body):
    body(0, 0, True, False)
    with eng.Fori(0, B // 2 - 1) as i:
        body(2 * i + 1, 1, False, False)
        body(2 * i + 2, 0, False, False)
    body(B - 1, 1, False, True)


def behind(b, k, lag, first):
    n = k - lag
    if n >= UNITS or (n < 0 and first):
        return None
    return (b, n) if n >= 0 else (b - 1, n + UNITS)


def program(nc, t, out):
    with ExitStack() as ctx:
        def sb(name, shape, dt=F32):
            return ctx.enter_context(nc.sbuf_tensor(name, shape, dt))

        mem = {
            "X": sb("X", [P, NT, P]),
            "XN": sb("XN", [P, NT, P]),
            "G": sb("G", [P, 8, B, P]),
            "modT": sb("modT", [P, 4, B]),
            "ident": sb("ident", [P, P]),
            "ones": sb("ones", [1, P]),
            "slot": sb("slot", [P, 2, NT + TB], U32),
            "logit": sb("logit", [P, NT, E]),
            "share": sb("share", [P, 2, NT]),
            "WgT": sb("WgT", [P, FI]),
            "WuT": sb("WuT", [P, FI]),
            "WdT": sb("WdT", [P, 3, P]),
            "buf": nc.dram_tensor("expert_in", [SLOTS + 2 * B * S, P], F32),
            "y": nc.dram_tensor("expert_out", [SLOTS, P], F32),
        }
        banks = [ctx.enter_context(nc.psum_tensor(f"bank{i}", [P, 512], F32)) for i in range(8)]
        setup(nc, t, mem, banks)
        attention_rel(nc, t, mem, banks)
        route(nc, t, mem, banks)
        experts(nc, t, mem, banks)
        ffn_weights(nc, t, mem, banks)
        attention_causal(nc, t, mem, banks, out)


def setup(nc, t, mem, banks):
    with ExitStack() as ctx:
        def sb(name, shape, dt=F32):
            return ctx.enter_context(nc.sbuf_tensor(name, shape, dt))

        def sem(name):
            return ctx.enter_context(nc.semaphore(name))

        X, G, modT, ident, ones = (mem[k] for k in ("X", "G", "modT", "ident", "ones"))
        cT = sb("cT", [P, 2, B])
        scT = sb("scT", [P, 2, B])
        wmod = sb("wmod", [P, 2, 6 * P])
        rows = sb("mod_rows", [B, 2, 6, P])
        sign = sb("gate_sign", [B, P])
        mag = sb("gate_size", [B, P])
        scratch = nc.dram_tensor("mod_rows_dram", [8, B, P], F32)
        x_in, c_in, w_in = sem("x_in"), sem("c_in"), sem("wmod_in")
        silu_done, modT_done, rows_done = sem("silu_done"), sem("modT_done"), sem("rows_done")
        rows_copied, rows_ready, modT_copied = sem("rows_copied"), sem("rows_ready"), sem("modT_copied")
        rows_stored, spread = sem("rows_stored"), sem("rows_spread")
        dve_step = sem("setup_dve_step")
        zeros = sb("zeros", [P, ET, P])
        zero_ready, zeroed = sem("zero_ready"), sem("slots_zeroed")
        block = ctx.enter_context(nc.Block())

        @block.sync
        def _(sp):
            for layer in range(2):
                sp.dma_start(cT[:, layer, :], t[f"c{layer}T"]).then_inc(c_in, 16)
                sp.dma_start(wmod[:, layer, :], t[f"L{layer}_wmod"]).then_inc(w_in, 16)
            sp.dma_start(ident[:], t["ident"]).then_inc(x_in, 16)
            sp.dma_start(ones[:], t["ones"]).then_inc(x_in, 16)
            sp.dma_start(X[:], t["x"].rearrange("(t p) d -> p t d", p=P)).then_inc(x_in, 16)
            sp.wait_ge(rows_ready, 1)
            for layer in range(2):
                for kind, part in ((GA0, 2), (CB0, 4), (SB0, 3), (GB0, 5)):
                    sp.dma_start(scratch.ap()[4 * layer + kind], rows[:, layer, part, :]).then_inc(rows_stored, 16)
            sp.wait_ge(rows_stored, 8 * 16)
            for kind in range(8):
                sp.dma_start(G[:, kind, :, :].rearrange("p b d -> p (b d)"),
                             scratch.ap()[kind].rearrange("b d -> (b d)").partition_broadcast(P)).then_inc(spread, 16)
            sp.wait_ge(spread, 8 * 16)
            sp.wait_ge(x_in, 3 * 16)

        @block.gpsimd
        def _(pool):
            pool.memset(zeros[:], 0.0).then_inc(zero_ready, 1)
            pool.wait_ge(zero_ready, 1)
            for e in range(E):
                pool.dma_start(mem["buf"].ap()[e * CAP:(e + 1) * CAP].rearrange("(p c) d -> p c d", p=P), zeros[:]
                               ).then_inc(zeroed, 16)
            pool.wait_ge(zeroed, E * 16)

        @block.scalar
        def _(act):
            act.wait_ge(c_in, 32)
            act.activation(scT[:], cT[:], ACT.Silu).then_inc(silu_done, 1)

        @block.tensor
        def _(pe):
            pe.wait_ge(silu_done, 1)
            pe.wait_ge(w_in, 32)
            for layer in range(2):
                for n, part in enumerate((1, 0)):
                    k = 2 * layer + n
                    mm = pe.matmul(banks[4][:, k * B:(k + 1) * B], wmod[:, layer, part * P:(part + 1) * P],
                                   scT[:, layer, :], start=True, stop=True)
            mm.then_inc(modT_done, 1)
            for layer in range(2):
                for half in range(2):
                    mm = pe.matmul(banks[2 * layer + half][0:B, 0:3 * P], scT[:, layer, :],
                                   wmod[:, layer, half * 3 * P:(half + 1) * 3 * P], start=True, stop=True)
            mm.then_inc(rows_done, 1)

        @block.vector
        def _(dve):
            own = Chain(dve, dve_step)
            dve.wait_ge(modT_done, 1)
            for layer in range(2):
                k = 2 * layer
                own.step(dve.tensor_scalar(modT[:, k, :], banks[4][:, k * B:(k + 1) * B], 1.0, None, ALU.add))
                own.step(dve.tensor_copy(modT[:, k + 1, :], banks[4][:, (k + 1) * B:(k + 2) * B]))
            dve.wait_ge(rows_done, 1)
            for layer in range(2):
                for half in range(2):
                    own.step(dve.tensor_copy(rows[:, layer, 3 * half:3 * half + 3, :],
                                             banks[2 * layer + half][0:B, 0:3 * P].rearrange("b (k d) -> b k d", k=3)))
            own.join()
            for layer in range(2):
                own.link(dve.tensor_scalar(rows[:, layer, 4, :], rows[:, layer, 4, :], 1.0, None, ALU.add))
                for part in (2, 5):
                    g = rows[:, layer, part, :]
                    own.link(dve.tensor_scalar(sign[:], g, 0.0, 2.0, ALU.is_ge, ALU.mult))
                    own.link(dve.tensor_scalar(sign[:], sign[:], -1.0, None, ALU.add))
                    own.link(dve.tensor_scalar(mag[:].bitcast(I32), g.bitcast(I32), 0x7FFFFFFF, None, ALU.bitwise_and))
                    own.link(dve.tensor_scalar(mag[:], mag[:], 0.25, None, ALU.max))
                    own.link(dve.tensor_tensor(g, mag[:], sign[:], ALU.mult))
            dve.memset(sign[:], 0.0).then_inc(rows_ready, 1)


def attention_rel(nc, t, mem, banks):
    with ExitStack() as ctx:
        def sb(name, shape, dt=F32):
            return ctx.enter_context(nc.sbuf_tensor(name, shape, dt))

        def sem(name):
            return ctx.enter_context(nc.semaphore(name))

        X, XN, G, modT, ident, ones = (mem[k] for k in ("X", "XN", "G", "modT", "ident", "ones"))
        W = {k: sb(f"{k}_sb", [P, P]) for k in ("WqT", "WkT", "WvT", "WoT", "WqdT")}
        WrT = sb("WrT_sb", [P, E])
        gamma, beta = sb("gamma_b", [P, P]), sb("beta_b", [P, P])
        bq, bk, bv = (sb(k, [P, 1]) for k in ("bq_sb", "bk_sb", "bv_sb"))
        bqd, bo = sb("bqd_sb", [1, P]), sb("bo_sb", [1, P])
        EK = sb("EK", [P, 496])
        VR = sb("VR", [P, 2, 2, NJ, 64 + QB * DH])
        head_mask = sb("head_mask", [P, 2, HG])
        pick = sb("pick", [P, HG + QB])
        half_neg = sb("half_neg", [P, TB])
        stats, mv = sb("stats", [P, TB, 6]), sb("mv", [P, TB, 2])
        var, rstd = sb("var", [P, TB]), sb("rstd", [P, TB])
        xn = sb("xn", [P, TB, P])
        HT = sb("HT", [P, S])
        qT = sb("qT", [P, S])
        q_tok = sb("q_tok", [P, TB, P])
        keys = sb("keys", [P, 2, 4, S])
        V = sb("V", [P, 2, TB, P])
        Qc = sb("Qc", [P, 2, NJ, QB, HG])
        Qr = sb("Qr", [P, 2, NJ, QB, HG])
        negmax = sb("negmax", [P, 4, 2])
        probs = sb("probs", [P, 4, 2, S])
        sums = sb("sums", [P, 2, 2, NJ])
        inv = sb("inv", [P, 2, NJ])
        pT = sb("pT", [P, 2, 2, 2, P])
        om = sb("om", [P, 2, 2, (HG + QB) * DH])
        o8 = sb("o8", [P, 2, 2, NJ, DH])
        o_tok = sb("o_tok", [P, TB, P])
        oT = sb("oT", [P, S])
        gated = sb("gated", [P, TB, P])
        stage = sb("stage", [P, TB, P])
        rstats, rmv = sb("route_stats", [P, TB, 6]), sb("route_mv", [P, TB, 2])
        rvar, rrstd = sb("route_var", [P, TB]), sb("route_rstd", [P, TB])
        xnT = sb("xnT", [P, TB, P])
        q_dram = nc.dram_tensor("queries_dram", [2, S, P], F32)
        o_dram = nc.dram_tensor("outputs_dram", [2, P, 2 * NJ * DH], F32)

        S_bank, PT_bank, O_bank = banks[0:2], banks[2], banks[3:5]
        A_bank, C_bank, R_bank = banks[5], banks[6], banks[7]
        FIRST_BLOCK = (0, 0, 64, 128)
        LAST_BLOCK = (128, 192, S, S)

        w_in = sem("attn_weights_in")
        rv_in, rv_ready, qr_clear = sem("rv_in"), sem("rv_ready"), sem("qr_clear")
        const_ready = sem("half_neg_ready")
        seen = sem("ln_seen")
        ln_step, ln_var, ln_rstd, xn_ready = sem("ln_step"), sem("ln_var"), sem("ln_rstd"), sem("xn_ready")
        a_full, a_free = sem("a_full"), sem("a_free")
        ht_ready, q_ready, k_ready, v_ready, q_tok_ready = (
            sem(n) for n in ("ht_ready", "q_ready", "k_ready", "v_ready", "q_tok_ready"))
        sp_seen = sem("sp_seen")
        q_sent, qr_in = sem("q_sent"), [sem(f"qr_in{s}") for s in range(2)]
        qc_ready, keys_ready, vr_ready, vr_wait = (sem(n) for n in ("qc_ready", "keys_ready", "vr_ready", "vr_wait"))
        scores_done, max_done, exp_done = sem("scores_done"), sem("max_done"), sem("exp_done")
        turned, pT_ready, pv_done = sem("turned"), sem("pT_ready"), sem("pv_done")
        masked, summed, inv_done, normed = sem("masked"), sem("summed"), sem("inv_done"), sem("normed")
        o_sent, o_back = sem("o_sent"), sem("o_back")
        oT_full, oT_ready, y_full, y_gated, x_done = (
            sem(n) for n in ("oT_full", "oT_ready", "y_full", "y_gated", "x_done"))
        r_step, r_var, r_rstd, r_ready, r_turned, r_copied, r_full, r_read = (
            sem(n) for n in ("route_step", "route_var_ready", "route_rstd_ready", "route_xn_ready", "route_turned",
                             "route_copied", "route_full", "route_read"))
        block = ctx.enter_context(nc.Block())

        LOADS = 5 + 3 + 3 + 2 + 2 + QB
        PROJECT_AT = (3, 4, 5)
        FINISH_AT = (8, 9)
        ROUTE_AT = (10, 11, 13, 14)

        @block.sync
        def _(sp):
            loads = [(W[k][:], t[k]) for k in W]
            loads += [(gamma[:], t["gamma"].partition_broadcast(P)), (beta[:], t["beta"].partition_broadcast(P)),
                      (WrT[:], t["WrT"])]
            loads += [(bq[:], t["bq"].unsqueeze(1)), (bk[:], t["bk"].unsqueeze(1)), (bv[:], t["bv"].unsqueeze(1)),
                      (bo[:], t["bo"].unsqueeze(0)), (bqd[:], t["bqd"])]
            loads += [(head_mask[:], t["head_mask"]), (pick[:], t["pick"])]
            for q in range(QB):
                loads.append((EK[q * DH:(q + 1) * DH, :], t["ek_ext"][:, QB - 1 - q:QB - 1 - q + 496]))
            assert len(loads) == LOADS
            for dst, src in loads:
                sp.dma_start(dst, src).then_inc(w_in, 16)

            def store_queries(b, par):
                sp.wait_ge(q_tok_ready, b + 1)
                sp.dma_start(q_dram.ap()[par].rearrange("(c p) n -> p c n", p=P), q_tok[:]).then_inc(q_sent, 16)
                sp.wait_ge(q_sent, 16 * b + 16)
                sp.sem_inc(sp_seen, 1)

            def place_queries(b, par, s):
                if isinstance(b, int) and b == 0:
                    sp.wait_ge(qr_clear, 1)
                else:
                    sp.wait_ge(scores_done, UNITS * b - 8 + 8 * s)
                src = q_dram.ap()[par].rearrange("(j q) (d s h) -> q d s j h", q=QB, d=DH, s=2)
                for q in range(QB):
                    sp.dma_start(Qr[q * DH:(q + 1) * DH, s, :, q, :], src[q, :, s, :, :]).then_inc(qr_in[s], 16)

            def gather_outputs(b, par):
                sp.wait_ge(normed, 2 * b + 2)
                sp.dma_start(o_dram.ap()[par], o8[:, par, :, :, :].rearrange("p s j d -> p (s j d)")).then_inc(o_sent, 16)
                sp.wait_ge(o_sent, 16 * b + 16)
                sp.sem_inc(sp_seen, 1)
                sp.wait_ge(oT_full, b + 1)
                src = o_dram.ap()[par].rearrange("(q h) (s j d) -> j q s h d", h=HG, s=2, d=DH)
                for j in range(NJ):
                    c, at = j // HG, (j % HG) * QB
                    for s in range(2):
                        sp.dma_start(o_tok[at:at + QB, c, 64 * s:64 * s + 64].rearrange("p (h d) -> p h d", d=DH),
                                     src[j, :, s, :, :]).then_inc(o_back, 16)

            def batch(b, par, first, last):
                if not first:
                    place_queries(b, par, 1)
                    gather_outputs(b - 1, 1 - par)
                if not last:
                    store_queries(b + 1, 1 - par)
                    place_queries(b + 1, 1 - par, 0)

            store_queries(0, 0)
            for s in range(2):
                place_queries(0, 0, s)
            every_batch(sp, batch)
            gather_outputs(B - 1, 1)

        @block.tensor
        def _(pe):
            def project(b, k):
                pe.wait_ge(a_free, 3 * b + k + 1)
                if k == 0:
                    pe.wait_ge(xn_ready, b + 1)
                    for c in range(TB):
                        mm = pe.transpose(A_bank[:, c * P:(c + 1) * P], xn[:, c, :], ident[:])
                elif k == 1:
                    pe.wait_ge(ht_ready, b + 1)
                    pe.matmul(A_bank[:, 0:S], W["WqT"][:], HT[:], start=True, stop=True)
                    mm = pe.matmul(A_bank[:, S:2 * S], W["WkT"][:], HT[:], start=True, stop=True)
                else:
                    for c in range(TB):
                        h = HT[:, c * P:(c + 1) * P]
                        pe.matmul(A_bank[:, c * P:(c + 1) * P], h, W["WvT"][:], start=True, stop=True)
                        q = A_bank[:, S + c * P:S + (c + 1) * P]
                        pe.matmul(q, h, W["WqdT"][:], start=True, stop=False)
                        mm = pe.matmul(q, ones[:], bqd[:], start=False, stop=True)
                mm.then_inc(a_full, 1)

            def scores(b, par, u):
                s, jp = u // 8, u % 8
                if u % 8 == 0:
                    pe.wait_ge(qc_ready, 2 * b + s + 1)
                    pe.wait_ge(qr_in[s], (b + 1) * QB * 16)
                    pe.wait_ge(keys_ready, b + 1)
                pe.wait_ge(exp_done, b * UNITS + u + 1)
                for jj in range(2):
                    j = 2 * jp + jj
                    g = j // 4
                    lo, hi = FIRST_BLOCK[g], LAST_BLOCK[g]
                    at = jj * S
                    pe.matmul(S_bank[u % 2][:, at:at + S], Qc[:, s, j, :, :].rearrange("p q h -> p (q h)"),
                              keys[:, par, g, :], start=True, stop=False)
                    mm = pe.matmul(S_bank[u % 2][:, at + lo:at + hi], Qr[:, s, j, :, :].rearrange("p q h -> p (q h)"),
                                   EK[:, 240 - QB * j + lo:240 - QB * j + hi], start=False, stop=True)
                mm.then_inc(scores_done, 1)

            def turn(b, u):
                pe.wait_ge(exp_done, b * UNITS + u + 3)
                pe.wait_ge(pT_ready, b * UNITS + u + 2)
                for jj in range(2):
                    for c in range(2):
                        n = 2 * jj + c
                        mm = pe.transpose(PT_bank[:, n * P:(n + 1) * P], probs[:, u % 4, jj, c * P:(c + 1) * P], ident[:])
                mm.then_inc(turned, 1)

            def mix(b, u):
                s, jp = u // 8, u % 8
                if u % 8 == 0:
                    pe.wait_ge(vr_ready, 4 * b + 2 * s + 2)
                pe.wait_ge(pT_ready, b * UNITS + u + 3)
                pe.wait_ge(masked, b * UNITS + u + 1)
                for jj in range(2):
                    j = 2 * jp + jj
                    for c in range(2):
                        mm = pe.matmul(O_bank[u % 2][:, jj * 192:(jj + 1) * 192], pT[:, u % 2, jj, c, :],
                                       VR[:, s, c, j, :], start=(c == 0), stop=(c == 1))
                mm.then_inc(pv_done, 1)

            def finish(b, k):
                if k == 0:
                    pe.wait_ge(o_back, (b + 1) * 2 * NJ * 16)
                    pe.wait_ge(y_gated, b + 1)
                    for c in range(TB):
                        mm = pe.transpose(C_bank[:, c * P:(c + 1) * P], o_tok[:, c, :], ident[:])
                    mm.then_inc(oT_full, 1)
                else:
                    pe.wait_ge(oT_ready, b + 1)
                    for c in range(TB):
                        dst = C_bank[:, c * P:(c + 1) * P]
                        pe.matmul(dst, oT[:, c * P:(c + 1) * P], W["WoT"][:], start=True, stop=False)
                        mm = pe.matmul(dst, ones[:], bo[:], start=False, stop=True)
                    mm.then_inc(y_full, 1)

            def route(b, k):
                if k == 2:
                    pe.wait_ge(r_ready, b + 1)
                    pe.wait_ge(r_read, b + 1)
                    for c in range(TB):
                        mm = pe.transpose(R_bank[:, c * P:(c + 1) * P], stage[:, c, :], ident[:])
                    mm.then_inc(r_turned, 1)
                if k == 3:
                    pe.wait_ge(r_copied, b + 1)
                    for c in range(TB):
                        mm = pe.matmul(R_bank[:, S + c * E:S + (c + 1) * E], xnT[:, c, :], WrT[:], start=True, stop=True)
                    mm.then_inc(r_full, 1)

            def batch(b, par, first, last):
                for k in range(UNITS + (3 if last else 0)):
                    if k < UNITS:
                        scores(b, par, k)
                    if behind(b, k, 2, first):
                        turn(*behind(b, k, 2, first))
                    if behind(b, k, 3, first):
                        mix(*behind(b, k, 3, first))
                    if not last and k in PROJECT_AT:
                        project(b + 1, PROJECT_AT.index(k))
                    if not first and k in FINISH_AT:
                        finish(b - 1, FINISH_AT.index(k))
                    if not first and k in ROUTE_AT:
                        route(b - 1, ROUTE_AT.index(k))

            pe.wait_ge(w_in, 16 * LOADS)
            for k in range(3):
                project(0, k)
            every_batch(pe, batch)
            for k in range(2):
                finish(B - 1, k)
            for k in range(4):
                route(B - 1, k)

        @block.gpsimd
        def _(pool):
            def power(ready, n, v, r, done):
                pool.wait_ge(ready, n + 1)
                pool.tensor_tensor(r[:], v[:], half_neg[:], ALU.pow).then_inc(done, 1)

            def far_keys(b, par):
                pool.wait_ge(k_ready, b + 1)
                for g in range(4):
                    cols = slice(LAST_BLOCK[g], S) if g < 2 else slice(0, FIRST_BLOCK[g])
                    n = cols.stop - cols.start
                    edge = EK[:, 495:496] if g < 2 else EK[:, 0:1]
                    ins = pool.tensor_tensor(keys[:, par, g, cols], keys[:, par, g, cols], edge.broadcast_to([P, n]), ALU.add)
                ins.then_inc(keys_ready, 1)

            def spread_queries(b, s):
                pool.wait_ge(q_ready, b + 1)
                if not isinstance(b, int) or b:
                    pool.wait_ge(scores_done, UNITS * b - 8 + 8 * s)
                pool.tensor_tensor(Qc[:, s, :, :, :].rearrange("p j q h -> p (j q) h"),
                                   qT[:].unsqueeze(2).broadcast_to([P, S, HG]),
                                   head_mask[:, s, :].unsqueeze(1).broadcast_to([P, S, HG]), ALU.mult).then_inc(qc_ready, 1)

            def spread_values(b, par, s):
                pool.wait_ge(v_ready, b + 1)
                if not isinstance(b, int) or b:
                    pool.wait_ge(pv_done, b * UNITS - 8 + 8 * s + 2)
                pool.sem_inc(vr_wait, 1)
                for c in range(2):
                    pool.tensor_copy(VR[:, s, c, :, 0:64],
                                     V[:, par, c, 64 * s:64 * s + 64].unsqueeze(1).broadcast_to([P, NJ, 64])
                                     ).then_inc(vr_ready, 1)

            def batch(b, par, first, last):
                if not last:
                    power(ln_var, b + 1, var, rstd, ln_rstd)
                if not first:
                    spread_queries(b, 1)
                    spread_values(b, par, 1)
                if not last:
                    far_keys(b + 1, 1 - par)
                    spread_queries(b + 1, 0)
                if not first:
                    power(r_var, 2 * (b - 1), rvar, rrstd, r_rstd)
                    power(r_var, 2 * (b - 1) + 1, rvar, rrstd, r_rstd)
                if not last:
                    spread_values(b + 1, 1 - par, 0)

            pool.memset(half_neg[:], -0.5).then_inc(const_ready, 1)
            pool.memset(Qr[:], 0.0).then_inc(const_ready, 1)
            pool.wait_ge(const_ready, 2)
            pool.sem_inc(qr_clear, 1)
            rv = t["rv_ext"]
            for c in range(2):
                for j in range(NJ):
                    pool.dma_start(VR[:, 0, c, j, 64:64 + P], bass.AP(rv.tensor, (15 + 8 * c - j) * P, [[DH, P], [1, P]])
                                   ).then_inc(rv_in, 16)
            power(ln_var, 0, var, rstd, ln_rstd)
            pool.wait_ge(w_in, 16 * LOADS)
            far_keys(0, 0)
            for s in range(2):
                spread_queries(0, s)
            pool.wait_ge(rv_in, 2 * NJ * 16)
            pool.tensor_copy(VR[:, 1, :, :, 64:64 + P], VR[:, 0, :, :, 64:64 + P]).then_inc(rv_ready, 1)
            spread_values(0, 0, 0)
            spread_values(0, 0, 1)
            every_batch(pool, batch)
            power(r_var, 2 * (B - 1), rvar, rrstd, r_rstd)
            power(r_var, 2 * (B - 1) + 1, rvar, rrstd, r_rstd)

        @block.scalar
        def _(act):
            def project(b, par, k):
                act.wait_ge(a_full, 3 * b + k + 1)
                if k == 0:
                    act.activation(HT[:], A_bank[:, 0:S], ACT.Identity, bias=modT[:, 1, bass.ds(b, 1)],
                                   scale=modT[:, 0, bass.ds(b, 1)]).then_inc(ht_ready, 1)
                    act.wait_ge(ht_ready, b + 1)
                elif k == 1:
                    if not isinstance(b, int) or b:
                        act.wait_ge(qc_ready, 2 * b)
                    act.activation(qT[:], A_bank[:, 0:S], ACT.Identity, bias=bq[:]).then_inc(q_ready, 1)
                    act.activation(keys[:, par, :, :], A_bank[:, S:2 * S].unsqueeze(1).broadcast_to([P, 4, S]),
                                   ACT.Identity, bias=bk[:]).then_inc(k_ready, 1)
                    act.wait_ge(k_ready, b + 1)
                else:
                    if not isinstance(b, int) or b:
                        act.wait_ge(q_sent, 16 * b)
                    act.activation(q_tok[:], A_bank[:, S:2 * S].rearrange("p (c d) -> p c d", c=TB),
                                   ACT.Identity).then_inc(q_tok_ready, 1)
                    act.activation(V[:, par, :, :], A_bank[:, 0:S].rearrange("p (c d) -> p c d", c=TB),
                                   ACT.Identity).then_inc(v_ready, 1)
                    act.wait_ge(v_ready, b + 1)
                act.sem_inc(a_free, 1)

            def exponent(b, par, u):
                s, jp = u // 8, u % 8
                if u == 0:
                    act.wait_ge(inv_done, 2 * b + 1)
                act.wait_ge(max_done, b * UNITS + u + 1)
                act.wait_ge(turned, b * UNITS + u + 1)
                for jj in range(2):
                    j = 2 * jp + jj
                    a = act.activation(probs[:, u % 4, jj, :], S_bank[u % 2][:, jj * S:(jj + 1) * S], ACT.Exp,
                                       bias=negmax[:, u % 4, jj:jj + 1], accum_out=sums[:, par, s, j:j + 1])
                a.then_inc(exp_done, 1)

            def copy_turned(b, u):
                act.wait_ge(turned, b * UNITS + u + 5)
                act.wait_ge(pv_done, b * UNITS + u + 1)
                act.activation(pT[:, u % 2, :, :, :], PT_bank[:].rearrange("p (j c n) -> p j c n", j=2, c=2),
                               ACT.Identity).then_inc(pT_ready, 1)

            def finish(b):
                act.wait_ge(oT_full, b + 2)
                act.activation(oT[:], C_bank[:, 0:S], ACT.Identity, bias=bv[:]).then_inc(oT_ready, 1)

            def route(b):
                act.wait_ge(r_turned, b + 1)
                act.activation(xnT[:], R_bank[:, 0:S].rearrange("p (c d) -> p c d", c=TB), ACT.Identity).then_inc(r_copied, 1)

            def batch(b, par, first, last):
                for k in range(UNITS + (3 if last else 0)):
                    if behind(b, k, 1, first):
                        bb, u = behind(b, k, 1, first)
                        exponent(bb, par if k else 1 - par, u)
                    if behind(b, k, 2, first):
                        copy_turned(*behind(b, k, 2, first))
                    if not last and k in PROJECT_AT:
                        project(b + 1, 1 - par, PROJECT_AT.index(k))
                    if not first and k == FINISH_AT[0]:
                        finish(b - 1)
                    if not first and k == ROUTE_AT[2]:
                        route(b - 1)

            act.sem_inc(exp_done, 2)
            act.sem_inc(turned, 4)
            act.sem_inc(pT_ready, 2)
            act.sem_inc(pv_done, 2)
            act.sem_inc(a_free, 1)
            act.sem_inc(oT_full, 1)
            act.wait_ge(w_in, 16 * LOADS)
            for k in range(3):
                project(0, 0, k)
            every_batch(act, batch)
            finish(B - 1)
            route(B - 1)

        @block.vector
        def _(dve):
            def moments(own, x, st, m, v):
                dve.sem_inc(seen, 1)
                for c in range(TB):
                    own.step(dve.bn_stats(st[:, c, :], x[:, c, :]))
                own.join()
                dve.sem_inc(seen, 1)
                for c in range(TB):
                    own.step(dve.bn_aggr(m[:, c, :], st[:, c, :]))
                own.join()
                own.link(dve.tensor_scalar(v[:], m[:, :, 1], EPS, None, ALU.add))

            def norm_in(b):
                own = Chain(dve, ln_step, 5, b)
                moments(own, X[:, bass.ds(TB * b, TB), :], stats, mv, var)
                dve.sem_inc(ln_var, 1)
                own.end()

            def norm_out(b):
                dve.wait_ge(ln_rstd, b + 1)
                for c in range(TB):
                    a = dve.tensor_scalar(xn[:, c, :], X[:, bass.ds(TB * b + c, 1), :].rearrange("p c d -> p (c d)"),
                                          mv[:, c, 0:1], rstd[:, c:c + 1], ALU.subtract, ALU.mult)
                a.then_inc(xn_ready, 1)

            def row_max(b, u):
                dve.wait_ge(scores_done, b * UNITS + u + 1)
                dve.tensor_reduce(negmax[:, u % 4, :], S_bank[u % 2][:].rearrange("p (j n) -> p j n", j=2),
                                  AX.X, ALU.max, negate=True).then_inc(max_done, 1)

            def diagonal(b, par, u):
                s, jp = u // 8, u % 8
                dve.wait_ge(pv_done, b * UNITS + u + 3)
                dve.tensor_tensor(
                    om[:, u % 2, :, :].rearrange("p j (g d) -> p j g d", d=DH),
                    O_bank[u % 2][:, 0:384].rearrange("p (j g d) -> p j g d", j=2, d=DH),
                    pick[:].unsqueeze(1).unsqueeze(3).broadcast_to([P, 2, HG + QB, DH]), ALU.mult).then_inc(masked, 1)
                dve.wait_ge(masked, b * UNITS + u + 3)
                dve.tensor_reduce(o8[:, par, s, 2 * jp:2 * jp + 2, :],
                                  om[:, u % 2, :, :].rearrange("p j (g d) -> p j d g", d=DH),
                                  AX.X, ALU.add).then_inc(summed, 1)

            def normalise(b, par, s):
                dve.wait_ge(exp_done, b * UNITS + 8 * s + 10)
                dve.reciprocal(inv[:, s, :], sums[:, par, s, :]).then_inc(inv_done, 1)
                dve.wait_ge(inv_done, 2 * b + s + 4)
                dve.wait_ge(summed, b * UNITS + 8 * s + 8)
                dve.tensor_tensor(o8[:, par, s, :, :], o8[:, par, s, :, :],
                                  inv[:, s, :].unsqueeze(2).broadcast_to([P, NJ, DH]), ALU.mult).then_inc(normed, 1)

            def finish(b):
                dve.wait_ge(y_full, b + 1)
                dve.tensor_tensor(gated[:], C_bank[:, 0:S].rearrange("p (c d) -> p c d", c=TB),
                                  G[:, GA0, bass.ds(b, 1), :].broadcast_to([P, TB, P]), ALU.mult).then_inc(y_gated, 1)
                dve.wait_ge(y_gated, b + 2)
                x = X[:, bass.ds(TB * b, TB), :]
                dve.tensor_tensor(x, x, gated[:], ALU.add).then_inc(x_done, 1)

            def route(b, k):
                own = Chain(dve, r_step, 17, b)
                own.at = (0, 5, 14, 17)[k]
                if k < 2:
                    if k == 0:
                        dve.wait_ge(x_done, b + 1)
                        moments(own, X[:, bass.ds(TB * b, TB), :], rstats, rmv, rvar)
                        dve.sem_inc(r_var, 1)
                    else:
                        dve.wait_ge(r_rstd, 2 * b + 1)
                        for c in range(TB):
                            own.step(dve.tensor_scalar(stage[:, c, :], X[:, bass.ds(TB * b + c, 1), :].rearrange("p c d -> p (c d)"),
                                                       rmv[:, c, 0:1], rrstd[:, c:c + 1], ALU.subtract, ALU.mult))
                        own.join()
                        for op, kind in ((ALU.mult, CB0), (ALU.add, SB0)):
                            own.link(dve.tensor_tensor(stage[:], stage[:], G[:, kind, bass.ds(b, 1), :].broadcast_to([P, TB, P]), op))
                        moments(own, stage, rstats, rmv, rvar)
                        dve.sem_inc(r_var, 1)
                elif k == 2:
                    dve.wait_ge(r_rstd, 2 * b + 2)
                    for c in range(TB):
                        a = dve.tensor_scalar(stage[:, c, :], stage[:, c, :], rmv[:, c, 0:1], rrstd[:, c:c + 1],
                                              ALU.subtract, ALU.mult)
                    own.link(a)
                    for op, row in ((ALU.mult, gamma), (ALU.add, beta)):
                        own.link(dve.tensor_tensor(stage[:], stage[:], row[:].unsqueeze(1).broadcast_to([P, TB, P]), op))
                    dve.tensor_copy(XN[:, bass.ds(TB * b, TB), :], stage[:]).then_inc(r_ready, 1)
                else:
                    dve.wait_ge(r_full, b + 1)
                    dve.tensor_copy(mem["logit"][:, bass.ds(TB * b, TB), :],
                                    R_bank[:, S:S + TB * E].rearrange("p (c e) -> p c e", e=E)).then_inc(r_read, 1)

            def batch(b, par, first, last):
                for k in range(UNITS + (4 if last else 0)):
                    item = behind(b, k, 4, first)
                    if item:
                        diagonal(item[0], par if k >= 4 else 1 - par, item[1])
                        if item[1] == 7:
                            normalise(item[0], par, 0)
                        if item[1] == 15:
                            normalise(item[0], par if k >= 4 else 1 - par, 1)
                    if k < UNITS:
                        row_max(b, k)
                    if not last and k == 0:
                        norm_in(b + 1)
                    if not last and k == 1:
                        norm_out(b + 1)
                    if not first and k == FINISH_AT[1]:
                        finish(b - 1)
                    if not first and k in ROUTE_AT:
                        route(b - 1, ROUTE_AT.index(k))

            dve.sem_inc(masked, 2)
            dve.sem_inc(y_gated, 1)
            dve.sem_inc(r_read, 1)
            dve.sem_inc(inv_done, 3)
            norm_in(0)
            norm_out(0)
            dve.wait_ge(w_in, 16 * LOADS)
            every_batch(dve, batch)
            finish(B - 1)
            for k in range(4):
                route(B - 1, k)


def route(nc, t, mem, banks):
    with ExitStack() as ctx:
        def sb(name, shape, dt=F32):
            return ctx.enter_context(nc.sbuf_tensor(name, shape, dt))

        def sem(name):
            return ctx.enter_context(nc.semaphore(name))

        XN = mem["XN"]
        order = sb("order", [P, E])
        before = sb("before", [P, P], BF16)
        all_ones = sb("all_ones", [P, P], BF16)
        spare = sb("spare", [P, 2, NT])
        wide = {k: sb(f"route_{k}", [P, NT, E]) for k in ("prob", "rest", "eq", "key", "sel1", "sel2", "rank", "tmp")}
        wide["logit"] = mem["logit"]
        sel = sb("route_sel", [P, NT, E], BF16)
        thin = {k: sb(f"route_{k}", [P, NT]) for k in ("max", "sum", "inv")}
        two = {k: sb(f"route_{k}", [P, 2, NT]) for k in ("best", "bestkey", "place", "kept", "base", "flat")}
        to = sb("route_to", [P, 2, NT], U32)
        w_in, sent = sem("route_in"), sem("tokens_sent")
        shifted, exped, sel_ready, rank_full, slots_ready = (
            sem(n) for n in ("logit_shifted", "logit_exped", "sel_ready", "rank_full", "slots_ready"))
        dve_step = sem("route_dve_step")
        block = ctx.enter_context(nc.Block())
        bufv = mem["buf"].ap()

        @block.sync
        def _(sp):
            for dst, src in ((order, "order"), (spare, "spare"), (before, "before"), (all_ones, "all_ones")):
                sp.dma_start(dst[:], t[src]).then_inc(w_in, 16)

        @block.tensor
        def _(pe):
            pe.wait_ge(w_in, 4 * 16)
            pe.wait_ge(sel_ready, 1)
            pe.matmul(banks[2][:, 0:NT * E], before[:], sel[:].rearrange("p t e -> p (t e)"), start=True, stop=False)
            for i in range(NT - 1):
                mm = pe.matmul(banks[2][:, (i + 1) * E:NT * E].rearrange("p (t e) -> p t e", e=E), all_ones[:],
                               sel[:, i, :].unsqueeze(1).broadcast_to([P, NT - 1 - i, E]),
                               start=False, stop=(i == NT - 2))
            mm.then_inc(rank_full, 1)

        @block.scalar
        def _(act):
            act.wait_ge(shifted, 1)
            act.activation(wide["prob"][:], wide["rest"][:], ACT.Exp).then_inc(exped, 1)

        @block.gpsimd
        def _(pool):
            pool.wait_ge(slots_ready, 1)
            for i in range(NT):
                for k in range(2):
                    pool.indirect_dma_start(
                        out=bufv, out_offset=bass.IndirectOffsetOnAxis(ap=to[:, k, i:i + 1], axis=0),
                        in_=XN[:, i, :], in_offset=None).then_inc(sent, 16)
            pool.wait_ge(sent, 2 * NT * 16)

        @block.vector
        def _(dve):
            dve.wait_ge(w_in, 4 * 16)
            own = Chain(dve, dve_step)
            over_e = lambda v: v.unsqueeze(2).broadcast_to([P, NT, E])
            over_t = lambda v: v.unsqueeze(1).broadcast_to([P, NT, E])
            w = {k: v[:] for k, v in wide.items()}
            own.link(dve.tensor_scalar(w["logit"], w["logit"], 10000.0, -10000.0, ALU.min, ALU.max))
            own.link(dve.tensor_reduce(thin["max"][:], w["logit"], AX.X, ALU.max))
            own.link(dve.tensor_tensor(w["rest"], w["logit"], over_e(thin["max"][:]), ALU.subtract))
            dve.sem_inc(shifted, 1)
            dve.wait_ge(exped, 1)
            own.link(dve.tensor_reduce(thin["sum"][:], w["prob"], AX.X, ALU.add))
            own.link(dve.tensor_scalar(thin["sum"][:], thin["sum"][:], 1e-12, None, ALU.add))
            own.link(dve.reciprocal(thin["inv"][:], thin["sum"][:]))
            own.link(dve.tensor_tensor(w["prob"], w["prob"], over_e(thin["inv"][:]), ALU.mult))
            src = w["prob"]
            for k in range(2):
                best, key, chosen = two["best"][:, k, :], two["bestkey"][:, k, :], w[f"sel{k + 1}"]
                own.link(dve.tensor_reduce(best, src, AX.X, ALU.max))
                own.link(dve.tensor_tensor(w["eq"], src, over_e(best), ALU.is_equal))
                own.link(dve.tensor_tensor(w["key"], w["eq"], over_t(order[:]), ALU.mult))
                own.link(dve.tensor_reduce(key, w["key"], AX.X, ALU.max))
                own.link(dve.tensor_tensor(chosen, w["key"], over_e(key), ALU.is_equal))
                if k == 0:
                    own.link(dve.scalar_tensor_tensor(out=w["rest"], in0=chosen, scalar=-2.0, in1=src,
                                                      op0=ALU.mult, op1=ALU.add))
                    src = w["rest"]
            dve.tensor_tensor(sel[:], w["sel1"], w["sel2"], ALU.add).then_inc(sel_ready, 1)
            dve.wait_ge(rank_full, 1)
            own.link(dve.tensor_copy(w["rank"], banks[2][:, 0:NT * E].rearrange("p (t e) -> p t e", e=E)))
            for k in range(2):
                own.link(dve.tensor_tensor(w["tmp"], w["rank"], w[f"sel{k + 1}"], ALU.mult))
                own.link(dve.tensor_reduce(two["place"][:, k, :], w["tmp"], AX.X, ALU.add))
            v = {k: a[:] for k, a in two.items()}
            own.link(dve.tensor_scalar(v["kept"], v["place"], float(CAP), None, ALU.is_lt))
            own.link(dve.tensor_tensor(mem["share"][:], v["best"], v["kept"], ALU.mult))
            own.link(dve.tensor_scalar(v["base"], v["bestkey"], -float(CAP), float(E * CAP), ALU.mult, ALU.add))
            own.link(dve.tensor_scalar(v["flat"], v["place"], float(CAP - 1), None, ALU.min))
            own.link(dve.tensor_tensor(v["flat"], v["flat"], v["base"], ALU.add))
            own.link(dve.memset(mem["slot"][:], 0))
            own.link(dve.tensor_copy(mem["slot"][:, :, 0:NT], v["flat"]))
            own.link(dve.tensor_tensor(v["flat"], v["flat"], spare[:], ALU.subtract))
            own.link(dve.tensor_tensor(v["flat"], v["flat"], v["kept"], ALU.mult))
            own.link(dve.tensor_tensor(v["flat"], v["flat"], spare[:], ALU.add))
            dve.tensor_copy(to[:], v["flat"]).then_inc(slots_ready, 1)


def experts(nc, t, mem, banks):
    with ExitStack() as ctx:
        def sb(name, shape, dt=F32):
            return ctx.enter_context(nc.sbuf_tensor(name, shape, dt))

        def sem(name):
            return ctx.enter_context(nc.semaphore(name))

        ident = mem["ident"]
        W12 = sb("W12_sb", [P, 2, 2 * FF])
        W3 = sb("W3_sb", [P, 2, FC, P])
        xe = sb("xe", [P, 2, ET, P])
        xeT = sb("xeT", [P, 2, CAP])
        silu = sb("silu_gate", [P, 2, CAP // 2])
        hT = sb("hT", [P, 2, FC, CAP])
        ye = sb("ye", [P, 2, ET, P])
        U = 2 * FC
        H = CAP // 2
        w_in = [sem(f"expert_w_in{p}") for p in range(2)]
        turned, xeT_ready = sem("xe_turned"), sem("xeT_ready")
        gu_full, silu_done, h_ready = sem("gu_full"), sem("silu_done"), sem("h_ready")
        y_full, y_ready, y_out = sem("ye_full"), sem("ye_ready"), [sem(f"ye_out{p}") for p in range(2)]
        up_done = sem("expert_done")
        xe_copy = sem("xe_copy_step")
        block = ctx.enter_context(nc.Block())
        bufv, yv = mem["buf"].ap(), mem["y"].ap()
        LOADS = 3

        @block.sync
        def _(sp):
            with sp.Fori(0, E // 2) as i:
                for p in range(2):
                    e = 2 * i + p
                    sp.wait_ge(up_done, e + 1)
                    sp.dma_start(xe[:, p, :, :], bufv[bass.ds(e * CAP, CAP)].rearrange("(c p) d -> p c d", p=P)
                                 ).then_inc(w_in[p], 16)
                    sp.dma_start(W12[:, p, :], t["W12T"][bass.ds(e, 1)].rearrange("e p f -> p (e f)")).then_inc(w_in[p], 16)
                    sp.dma_start(W3[:, p, :, :], t["W3T"][bass.ds(e, 1)].rearrange("e (c p) d -> p (e c) d", p=P)
                                 ).then_inc(w_in[p], 16)

        @block.tensor
        def _(pe):
            pe.sem_inc(up_done, 2)
            with pe.Fori(0, E // 2) as i:
                for p in range(2):
                    e = 2 * i + p
                    pe.wait_ge(w_in[p], (i + 1) * 16 * LOADS)
                    pe.wait_ge(xeT_ready, 2 * e + 2)
                    for c in range(ET):
                        mm = pe.transpose(banks[c // 4][:, (c % 4) * P:(c % 4 + 1) * P], xe[:, p, c, :], ident[:])
                    mm.then_inc(turned, 1)
                    pe.wait_ge(xeT_ready, 2 * e + 4)
                    for u in range(U):
                        f, half = u // 2, u % 2
                        pe.wait_ge(h_ready, e * U + u + 1)
                        for n in range(2):
                            mm = pe.matmul(banks[2 + 2 * (u % 2) + n][:, 0:H], W12[:, p, n * FF + f * P:n * FF + (f + 1) * P],
                                           xeT[:, p, half * H:(half + 1) * H], start=True, stop=True)
                        mm.then_inc(gu_full, 1)
                    pe.wait_ge(h_ready, e * U + U + 2)
                    pe.wait_ge(y_ready, e + 1)
                    for c in range(ET):
                        for f in range(FC):
                            mm = pe.matmul(banks[6 + c // 4][:, (c % 4) * P:(c % 4 + 1) * P], hT[:, p, f, c * P:(c + 1) * P],
                                           W3[:, p, f, :], start=(f == 0), stop=(f == FC - 1))
                    mm.then_inc(y_full, 1)
                    pe.wait_ge(y_full, e + 1)
                    pe.sem_inc(up_done, 1)

        @block.scalar
        def _(act):
            with act.Fori(0, E // 2) as i:
                for p in range(2):
                    e = 2 * i + p
                    act.wait_ge(turned, e + 1)
                    for n in range(2):
                        act.activation(xeT[:, p, n * 512:min(CAP, n * 512 + 512)], banks[n][:, 0:min(512, CAP - n * 512)],
                                       ACT.Identity).then_inc(xeT_ready, 1)
                    for u in range(U):
                        act.wait_ge(gu_full, e * U + u + 1)
                        act.activation(silu[:, u % 2, :], banks[2 + 2 * (u % 2)][:, 0:H], ACT.Silu).then_inc(silu_done, 1)
                    act.wait_ge(y_ready, e + 2)
                    act.dma_start(yv[bass.ds(e * CAP, CAP)].rearrange("(c p) d -> p c d", p=P), ye[:, p, :, :]
                                  ).then_inc(y_out[p], 16)
            for p in range(2):
                act.wait_ge(y_out[p], (E // 2) * 16 + 16)

        @block.vector
        def _(dve):
            dve.sem_inc(xeT_ready, 2)
            dve.sem_inc(h_ready, 2)
            dve.sem_inc(y_ready, 1)
            for p in range(2):
                dve.sem_inc(y_out[p], 16)
            with dve.Fori(0, E // 2) as i:
                for p in range(2):
                    e = 2 * i + p
                    for u in range(U):
                        f, half = u // 2, u % 2
                        dve.wait_ge(silu_done, e * U + u + 1)
                        dve.tensor_tensor(hT[:, p, f, half * H:(half + 1) * H], silu[:, u % 2, :],
                                          banks[3 + 2 * (u % 2)][:, 0:H], ALU.mult).then_inc(h_ready, 1)
                    dve.wait_ge(y_full, e + 1)
                    dve.wait_ge(y_out[p], i * 16 + 16)
                    dve.tensor_copy(ye[:, p, 0:4, :], banks[6][:].rearrange("p (c d) -> p c d", c=4)).then_inc(xe_copy, 1)
                    dve.tensor_copy(ye[:, p, 4, :], banks[7][:, 0:P]).then_inc(y_ready, 1)




def fp4_round(dve, own, x, q, amax, inv, size, low, n):
    blocks = lambda v: v.rearrange("p (b k) -> p b k", k=QBLK)
    wide = lambda v: v.unsqueeze(2).broadcast_to([v.shape[0], n // QBLK, QBLK])
    yield lambda: own.link(dve.tensor_scalar(size.bitcast(I32), x.bitcast(I32), 0x7FFFFFFF, None, ALU.bitwise_and))
    yield lambda: own.link(dve.tensor_reduce(amax, blocks(size), AX.X, ALU.max))
    yield lambda: own.link(dve.tensor_scalar(amax, amax, 1.0 / 6.0, 1e-12, ALU.mult, ALU.max))
    yield lambda: own.link(dve.reciprocal(inv, amax))
    yield lambda: own.link(dve.tensor_tensor(blocks(size), blocks(size), wide(inv), ALU.mult))
    yield lambda: own.link(dve.tensor_scalar(low, size, 0.25, None, ALU.is_gt))
    for mid in (0.75, 1.25, 1.75):
        yield lambda mid=mid: own.link(dve.scalar_tensor_tensor(out=low, in0=size, scalar=mid, in1=low,
                                                                op0=ALU.is_gt, op1=ALU.add))
    yield lambda: own.link(dve.tensor_scalar(low, low, 0.5, None, ALU.mult))
    for mid in (2.5, 3.5):
        yield lambda mid=mid: own.link(dve.scalar_tensor_tensor(out=low, in0=size, scalar=mid, in1=low,
                                                                op0=ALU.is_gt, op1=ALU.add))
    yield lambda: own.link(dve.tensor_scalar(size, size, 5.0, 2.0, ALU.is_gt, ALU.mult))
    yield lambda: own.link(dve.tensor_tensor(low, low, size, ALU.add))
    yield lambda: own.link(dve.scalar_tensor_tensor(out=low.bitcast(I32), in0=x.bitcast(I32), scalar=-0x80000000,
                                                    in1=low.bitcast(I32), op0=ALU.bitwise_and, op1=ALU.bitwise_or))
    yield lambda: own.link(dve.tensor_tensor(blocks(q), blocks(low), wide(amax), ALU.mult))


FP4_STEPS = 16


def ffn_weights(nc, t, mem, banks):
    with ExitStack() as ctx:
        def sb(name, shape, dt=F32):
            return ctx.enter_context(nc.sbuf_tensor(name, shape, dt))

        def sem(name):
            return ctx.enter_context(nc.semaphore(name))

        ident, WgT, WuT, WdT = (mem[k] for k in ("ident", "WgT", "WuT", "WdT"))
        N = 6 * P + FI
        raw = sb("w_raw", [P, N])
        size, low = sb("w_size", [P, N]), sb("w_low", [P, N])
        amax, inv = sb("w_amax", [P, N // QBLK]), sb("w_inv", [P, N // QBLK])
        w_in, cleared, w_ready, full = sem("ffn_w_in"), sem("ffn_w_cleared"), sem("ffn_w_ready"), sem("ffn_w_full")
        copied, step = sem("ffn_w_copied"), sem("ffn_w_step")
        block = ctx.enter_context(nc.Block())
        CH = [(0, P), (P, P), (2 * P, FI - 2 * P)]

        @block.sync
        def _(sp):
            sp.wait_ge(cleared, 1)
            for m, name in enumerate(("w_gate", "w_up")):
                w = t[name]
                at = 3 * m * P
                sp.dma_start(raw[:, at:at + 2 * P].rearrange("p (c k) -> p c k", c=2),
                             w[0:2 * P].rearrange("(c p) k -> p c k", p=P)).then_inc(w_in, 16)
                sp.dma_start(raw[0:FI - 2 * P, at + 2 * P:at + 3 * P], w[2 * P:FI]).then_inc(w_in, 16)
            sp.dma_start(raw[:, 6 * P:N], t["w_down"]).then_inc(w_in, 16)

        @block.vector
        def _(dve):
            dve.memset(raw[:], 0.0).then_inc(cleared, 1)
            own = Chain(dve, step)
            dve.wait_ge(w_in, 5 * 16)
            for do in fp4_round(dve, own, raw[:], raw[:], amax[:], inv[:], size[:], low[:], N):
                do()
            dve.sem_inc(w_ready, 1)
            for m, dst in enumerate((WgT, WuT)):
                dve.wait_ge(full, m + 1)
                dve.tensor_copy(dst[:], banks[m][:, 0:FI]).then_inc(copied, 1)
            dve.wait_ge(full, 3)
            dve.tensor_copy(WdT[:, 0:2, :], banks[2][:, 0:2 * P].rearrange("p (c n) -> p c n", c=2)).then_inc(copied, 1)
            dve.tensor_copy(WdT[0:FI - 2 * P, 2, :], banks[2][0:FI - 2 * P, 2 * P:3 * P]).then_inc(copied, 1)

        @block.tensor
        def _(pe):
            pe.wait_ge(w_ready, 1)
            for m in range(2):
                for at, w in CH:
                    mm = pe.transpose(banks[m][:, at:at + w], raw[0:w, 3 * m * P + at:3 * m * P + at + P], ident[0:w, 0:w])
                mm.then_inc(full, 1)
            for at, w in CH:
                mm = pe.transpose(banks[2][0:w, at:at + P], raw[:, 6 * P + at:6 * P + at + w], ident[:])
            mm.then_inc(full, 1)


def attention_causal(nc, t, mem, banks, out):
    with ExitStack() as ctx:
        def sb(name, shape, dt=F32):
            return ctx.enter_context(nc.sbuf_tensor(name, shape, dt))

        def sem(name):
            return ctx.enter_context(nc.semaphore(name))

        X, G, modT, ident = (mem[k] for k in ("X", "G", "modT", "ident"))
        slot, share = mem["slot"], mem["share"]
        WgT, WuT, WdT = (mem[k] for k in ("WgT", "WuT", "WdT"))
        Wq, Wk, Wv = (sb(f"L1_{k}", [P, P]) for k in ("Wq", "Wk", "Wv"))
        own_head = sb("own_head", [P, NH])
        causal = sb("causal", [P, 3, P])
        half_neg = sb("L1_half_neg", [P, TB])
        Y = sb("Y", [P, 2, TB, 2, P])
        index = sb("index", [P, 2, 2, TB], U32)
        y1 = sb("y1", [P, TB, P])
        stats, mv = sb("L1_stats", [P, TB, 6]), sb("L1_mv", [P, TB, 2])
        var, rstd = sb("L1_var", [P, TB]), sb("L1_rstd", [P, TB])
        xn = sb("L1_xn", [P, TB, P])
        HT = sb("L1_HT", [P, S])
        qT = sb("L1_qT", [P, 2, S])
        kT = sb("L1_kT", [P, S])
        V = sb("L1_V", [P, 2, TB, P])
        Km = sb("Km", [P, 2, NH, S])
        negmax = sb("L1_negmax", [P, 4, TB])
        probs = sb("L1_probs", [P, 2, TB, S])
        sums, inv = sb("L1_sums", [P, TB, NH]), sb("L1_inv", [P, TB, NH])
        pT = sb("L1_pT", [P, 2, 3, P])
        att = sb("L1_att", [P, TB, P])
        hn = sb("hn", [P, TB, P])
        fmv, fvar, frstd = sb("ffn_mv", [P, TB, 2]), sb("ffn_var", [P, TB]), sb("ffn_rstd", [P, TB])
        fstats = sb("ffn_stats", [P, TB, 6])
        hqT = sb("hqT", [P, TB, P])
        gate = sb("ffn_gate", [P, TB, FI])
        mid = sb("ffn_mid", [P, TB, FI])
        size, low = sb("ffn_size", [P, TB * FI]), sb("ffn_low", [P, TB * FI])
        amax, qinv = sb("ffn_amax", [P, TB * FI // QBLK]), sb("ffn_qinv", [P, TB * FI // QBLK])
        mT = sb("mT", [P, 2, 3, P])
        fy = sb("ffn_y", [P, TB, P])
        res = sb("res", [P, 2, TB, P])

        S_bank, PT_bank, O_bank = banks[0:2], banks[2], banks[3:5]
        A_bank, F_bank, U_bank = banks[5], banks[6], banks[7]
        CH = [(0, P), (P, P), (2 * P, FI - 2 * P)]
        NSTEP = UNITS + 2
        PROJECT = (9, 11, 12)
        FFN_AT = (5, 6, 7, 14, 15, 16)
        FJ, UJ = 5, 3

        w_in = sem("L1_w_in")
        gathered, index_ready = sem("y_gathered"), sem("index_ready")
        pool_seen = sem("L1_pool_seen")
        half_neg_ready = sem("L1_half_neg_ready")
        pre_step, seen = sem("L1_pre_step"), sem("L1_seen")
        var_ready, rstd_ready, xn_ready = sem("L1_var_ready"), sem("L1_rstd_ready"), sem("L1_xn_ready")
        a_full, a_free = sem("L1_a_full"), sem("L1_a_free")
        ht_ready, q_ready, k_ready, v_ready, km_ready = (
            sem(n) for n in ("L1_ht_ready", "L1_q_ready", "L1_k_ready", "L1_v_ready", "L1_km_ready"))
        scores_done, max_done, exp_done = sem("L1_scores_done"), sem("L1_max_done"), sem("L1_exp_done")
        turned, pT_ready, pv_done = sem("L1_turned"), sem("L1_pT_ready"), sem("L1_pv_done")
        att_step = sem("L1_att_step")
        fvar_ready, frstd_ready = sem("ffn_var_ready"), sem("ffn_rstd_ready")
        ffn_step = sem("ffn_step")
        h_ready, m_ready = sem("ffn_h_ready"), sem("ffn_m_ready")
        f_full, f_free = sem("f_full"), sem("f_free")
        u_full, u_free = sem("u_full"), sem("u_free")
        res_ready = sem("res_ready")
        stored = [sem(f"stored{p}") for p in range(2)]
        block = ctx.enter_context(nc.Block())
        out_v = out.rearrange("(b c p) d -> b p c d", c=TB, p=P)

        @block.sync
        def _(sp):
            for dst, src in ((Wq, "L1_Wq"), (Wk, "L1_Wk"), (Wv, "L1_Wv"), (own_head, "own_head"), (causal, "causal")):
                sp.dma_start(dst[:], t[src]).then_inc(w_in, 16)
            for p in range(2):
                sp.sem_inc(stored[p], 16)
            with sp.Fori(0, B // 2) as i:
                for p in range(2):
                    b = 2 * i + p
                    sp.wait_ge(res_ready, b + 1)
                    sp.dma_start(out_v[bass.ds(b, 1)].rearrange("b p c d -> p (b c) d"), res[:, p, :, :]).then_inc(stored[p], 16)
            for p in range(2):
                sp.wait_ge(stored[p], 16 + 16 * (B // 2))

        @block.tensor
        def _(pe):
            def project(b, par, k):
                pe.wait_ge(a_free, 3 * b + k + 1)
                if k == 0:
                    pe.wait_ge(xn_ready, b + 1)
                    for c in range(TB):
                        mm = pe.transpose(A_bank[:, c * P:(c + 1) * P], xn[:, c, :], ident[:])
                elif k == 1:
                    pe.wait_ge(ht_ready, b + 1)
                    pe.matmul(A_bank[:, 0:S], Wq[:], HT[:], start=True, stop=True)
                    mm = pe.matmul(A_bank[:, S:2 * S], Wk[:], HT[:], start=True, stop=True)
                else:
                    for c in range(TB):
                        mm = pe.matmul(A_bank[:, c * P:(c + 1) * P], HT[:, c * P:(c + 1) * P], Wv[:], start=True, stop=True)
                mm.then_inc(a_full, 1)

            def scores(b, par, h):
                if h == 0:
                    pe.wait_ge(q_ready, b + 1)
                    pe.wait_ge(km_ready, b + 1)
                pe.wait_ge(exp_done, b * UNITS + h + 1)
                for c in range(TB):
                    mm = pe.matmul(S_bank[h % 2][:, c * S:(c + 1) * S], qT[:, par, c * P:(c + 1) * P], Km[:, par, h, :],
                                   start=True, stop=True)
                mm.then_inc(scores_done, 1)

            def turn(b, h):
                pe.wait_ge(exp_done, b * UNITS + h + 3)
                pe.wait_ge(pT_ready, b * UNITS + h + 2)
                for n, (c, kc) in enumerate(((0, 0), (1, 1), (1, 0))):
                    mm = pe.transpose(PT_bank[:, n * P:(n + 1) * P], probs[:, h % 2, c, kc * P:(kc + 1) * P], ident[:])
                mm.then_inc(turned, 1)

            def mix(b, par, h):
                if h == 0:
                    pe.wait_ge(v_ready, b + 1)
                    pe.wait_ge(att_step, 4 * b + 1)
                pe.wait_ge(pT_ready, b * UNITS + h + 3)
                cols = slice(h * DH, (h + 1) * DH)
                O = O_bank[par]
                pe.matmul(O[:, cols], pT[:, h % 2, 0, :], V[:, par, 0, cols], start=True, stop=True)
                one = O[:, P + h * DH:P + (h + 1) * DH]
                pe.matmul(one, pT[:, h % 2, 2, :], V[:, par, 0, cols], start=True, stop=False)
                pe.matmul(one, pT[:, h % 2, 1, :], V[:, par, 1, cols], start=False, stop=True).then_inc(pv_done, 1)

            def ffn(b, k):
                if k < 5:
                    pe.wait_ge(f_free, FJ * b + k + 1)
                if k == 0:
                    pe.wait_ge(h_ready, b + 1)
                    for c in range(TB):
                        mm = pe.transpose(F_bank[:, c * P:(c + 1) * P], hn[:, c, :], ident[:])
                    mm.then_inc(f_full, 1)
                elif k in (1, 2):
                    c = k - 1
                    if c == 0:
                        pe.wait_ge(f_free, FJ * b + 2)
                    pe.matmul(F_bank[:, 0:FI], hqT[:, c, :], WgT[:], start=True, stop=True).then_inc(f_full, 1)
                    pe.wait_ge(u_free, UJ * b + c + 1)
                    pe.matmul(U_bank[:, 0:FI], hqT[:, c, :], WuT[:], start=True, stop=True).then_inc(u_full, 1)
                elif k in (3, 4):
                    c = k - 3
                    if c == 0:
                        pe.wait_ge(m_ready, b + 1)
                    for at, w in CH:
                        mm = pe.transpose(F_bank[0:w, at:at + P], mid[:, c, at:at + w], ident[:])
                    mm.then_inc(f_full, 1)
                else:
                    pe.wait_ge(f_free, FJ * b + 6)
                    pe.wait_ge(u_free, UJ * b + 3)
                    for c in range(TB):
                        for n, (at, w) in enumerate(CH):
                            mm = pe.matmul(U_bank[:, c * P:(c + 1) * P], mT[0:w, c, n, :], WdT[0:w, n, :],
                                           start=(n == 0), stop=(n == 2))
                    mm.then_inc(u_full, 1)

            def batch(b, par, last, first=False):
                for k in range(NSTEP):
                    if k < UNITS:
                        scores(b, par, k)
                    if 1 <= k <= UNITS:
                        turn(b, k - 1)
                    if k >= 2:
                        mix(b, par, k - 2)
                    if not last and k in PROJECT:
                        project(b + 1, 1 - par, PROJECT.index(k))
                    if not first and k in FFN_AT:
                        ffn(b - 1, FFN_AT.index(k))

            pe.wait_ge(w_in, 5 * 16)
            for k in range(3):
                project(0, 0, k)
            batch(0, 0, False, first=True)
            with pe.Fori(0, B // 2 - 1) as i:
                batch(2 * i + 1, 1, False)
                batch(2 * i + 2, 0, False)
            batch(B - 1, 1, True)
            for k in range(6):
                ffn(B - 1, k)

        @block.gpsimd
        def _(pool):
            def gather(b, par):
                pool.wait_ge(index_ready, b + 1)
                pool.sem_inc(pool_seen, 1)
                for c in range(TB):
                    for k in range(2):
                        pool.indirect_dma_start(out=Y[:, par, c, k, :], out_offset=None, in_=mem["y"].ap(),
                                                in_offset=bass.IndirectOffsetOnAxis(ap=index[:, par, k, c:c + 1], axis=0)
                                                ).then_inc(gathered, 16)

            def norm(b, ffn):
                ready, v, r, done = (fvar_ready, fvar, frstd, frstd_ready) if ffn else (var_ready, var, rstd, rstd_ready)
                pool.wait_ge(ready, b + 1)
                pool.tensor_tensor(r[:], v[:], half_neg[:], ALU.pow).then_inc(done, 1)

            def spread_keys(b, par):
                pool.wait_ge(k_ready, b + 1)
                for n in range(2):
                    hs = slice(n * HG, (n + 1) * HG)
                    ins = pool.tensor_tensor(Km[:, par, hs, :], kT[:].unsqueeze(1).broadcast_to([P, HG, S]),
                                             own_head[:, hs].unsqueeze(2).broadcast_to([P, HG, S]), ALU.mult)
                ins.then_inc(km_ready, 1)

            def batch(b, par, last, first=False):
                if not first:
                    norm(b - 1, True)
                if not last:
                    norm(b + 1, False)
                    gather(b + 2, par)
                    spread_keys(b + 1, 1 - par)

            pool.memset(half_neg[:], -0.5).then_inc(half_neg_ready, 1)
            pool.wait_ge(half_neg_ready, 1)
            gather(0, 0)
            norm(0, False)
            gather(1, 1)
            pool.wait_ge(w_in, 5 * 16)
            spread_keys(0, 0)
            batch(0, 0, False, first=True)
            with pool.Fori(0, B // 2 - 1) as i:
                batch(2 * i + 1, 1, False)
                batch(2 * i + 2, 0, False)
            batch(B - 1, 1, True)
            norm(B - 1, True)
            pool.wait_ge(gathered, (B + 1) * 4 * 16)

        @block.scalar
        def _(act):
            def project(b, par, k):
                act.wait_ge(a_full, 3 * b + k + 1)
                if k == 0:
                    act.activation(HT[:], A_bank[:, 0:S], ACT.Identity, bias=modT[:, 3, bass.ds(b, 1)],
                                   scale=modT[:, 2, bass.ds(b, 1)]).then_inc(ht_ready, 1)
                    act.wait_ge(ht_ready, b + 1)
                elif k == 1:
                    act.activation(qT[:, par, :], A_bank[:, 0:S], ACT.Identity, scale=float(DH) ** -0.5).then_inc(q_ready, 1)
                    if not isinstance(b, int) or b:
                        act.wait_ge(km_ready, b)
                    act.activation(kT[:], A_bank[:, S:2 * S], ACT.Identity).then_inc(k_ready, 1)
                    act.wait_ge(k_ready, b + 1)
                else:
                    act.activation(V[:, par, :, :], A_bank[:, 0:S].rearrange("p (c d) -> p c d", c=TB),
                                   ACT.Identity).then_inc(v_ready, 1)
                    act.wait_ge(v_ready, b + 1)
                act.sem_inc(a_free, 1)

            def exponent(b, h):
                if h == 0:
                    act.wait_ge(att_step, 4 * b + 2)
                act.wait_ge(max_done, b * UNITS + h + 1)
                act.wait_ge(turned, b * UNITS + h + 1)
                for c in range(TB):
                    a = act.activation(probs[:, h % 2, c, :], S_bank[h % 2][:, c * S:(c + 1) * S], ACT.Exp,
                                       bias=negmax[:, h % 4, c:c + 1], accum_out=sums[:, c, h:h + 1])
                a.then_inc(exp_done, 1)

            def ffn(b, k):
                act.wait_ge(f_full, FJ * b + k + 1)
                if k == 0:
                    act.activation(hqT[:], F_bank[:, 0:S].rearrange("p (c d) -> p c d", c=TB), ACT.Identity).then_inc(f_free, 1)
                elif k in (1, 2):
                    act.activation(gate[:, k - 1, :], F_bank[:, 0:FI], ACT.Silu).then_inc(f_free, 1)
                else:
                    c = k - 3
                    act.activation(mT[:, c, 0:2, :], F_bank[:, 0:S].rearrange("p (n d) -> p n d", n=2), ACT.Identity)
                    act.activation(mT[0:FI - 2 * P, c, 2, :], F_bank[0:FI - 2 * P, 2 * P:3 * P], ACT.Identity).then_inc(f_free, 1)

            def batch(b, par, last, first=False):
                for k in range(NSTEP):
                    if k < UNITS:
                        exponent(b, k)
                    if not last and k in PROJECT:
                        project(b + 1, 1 - par, PROJECT.index(k))
                    if not first and k in FFN_AT[0:5]:
                        ffn(b - 1, FFN_AT.index(k))

            act.sem_inc(exp_done, 2)
            act.sem_inc(turned, 2)
            act.sem_inc(a_free, 1)
            act.sem_inc(f_free, 1)
            act.wait_ge(w_in, 5 * 16)
            for k in range(3):
                project(0, 0, k)
            batch(0, 0, False, first=True)
            with act.Fori(0, B // 2 - 1) as i:
                batch(2 * i + 1, 1, False)
                batch(2 * i + 2, 0, False)
            batch(B - 1, 1, True)
            for k in range(5):
                ffn(B - 1, k)

        @block.vector
        def _(dve):
            def moments(own, x, st, m, v):
                dve.sem_inc(seen, 1)
                for c in range(TB):
                    own.step(dve.bn_stats(st[:, c, :], x[:, c, :]))
                own.join()
                dve.sem_inc(seen, 1)
                for c in range(TB):
                    own.step(dve.bn_aggr(m[:, c, :], st[:, c, :]))
                own.join()
                own.link(dve.tensor_scalar(v[:], m[:, :, 1], EPS, None, ALU.add))

            def prepare(b, par):
                own = Chain(dve, pre_step, 11, b)
                x = X[:, bass.ds(TB * b, TB), :]
                dve.wait_ge(gathered, (b + 1) * 4 * 16)
                dve.tensor_copy(index[:, 1 - par, :, :], slot[:, :, bass.ds(TB * b + TB, TB)]).then_inc(index_ready, 1)
                yv = Y[:, par, :, :, :]
                for c in range(TB):
                    own.step(dve.tensor_scalar(y1[:, c, :], yv[:, c, 0, :], share[:, 0, bass.ds(TB * b + c, 1)], None, ALU.mult))
                own.join()
                for c in range(TB):
                    own.step(dve.scalar_tensor_tensor(out=y1[:, c, :], in0=yv[:, c, 1, :], scalar=share[:, 1, bass.ds(TB * b + c, 1)],
                                                      in1=y1[:, c, :], op0=ALU.mult, op1=ALU.add))
                own.join()
                own.link(dve.tensor_tensor(y1[:], y1[:], G[:, GB0, bass.ds(b, 1), :].broadcast_to([P, TB, P]), ALU.mult))
                own.link(dve.tensor_tensor(x, x, y1[:], ALU.add))
                moments(own, x, stats, mv, var)
                own.end()
                dve.sem_inc(var_ready, 1)
                dve.wait_ge(rstd_ready, b + 1)
                if not isinstance(b, int) or b:
                    dve.wait_ge(a_full, 3 * b - 2)
                for c in range(TB):
                    a = dve.tensor_scalar(xn[:, c, :], x[:, c, :], mv[:, c, 0:1], rstd[:, c:c + 1], ALU.subtract, ALU.mult)
                a.then_inc(xn_ready, 1)

            def row_max(b, h):
                dve.wait_ge(scores_done, b * UNITS + h + 1)
                dve.tensor_reduce(negmax[:, h % 4, :], S_bank[h % 2][:].rearrange("p (c n) -> p c n", c=TB),
                                  AX.X, ALU.max, negate=True).then_inc(max_done, 1)

            def copy_turned(b, h):
                dve.wait_ge(turned, b * UNITS + h + 3)
                dve.wait_ge(pv_done, b * UNITS + h + 1)
                dve.tensor_tensor(pT[:, h % 2, :, :], PT_bank[:, 0:3 * P].rearrange("p (n d) -> p n d", n=3), causal[:],
                                  ALU.mult).then_inc(pT_ready, 1)

            def attended(b, par):
                own = Chain(dve, att_step, 4, b)
                own.at = 5
                x = X[:, bass.ds(TB * b, TB), :]
                dve.wait_ge(exp_done, b * UNITS + UNITS + 2)
                own.link(dve.reciprocal(inv[:], sums[:]))
                dve.wait_ge(pv_done, b * UNITS + UNITS + 2)
                own.link(dve.tensor_tensor(att[:].rearrange("p c (h d) -> p c h d", d=DH),
                                           O_bank[par][:, 0:S].rearrange("p (c h d) -> p c h d", c=TB, d=DH),
                                           inv[:].unsqueeze(3).broadcast_to([P, TB, NH, DH]), ALU.mult))
                own.link(dve.tensor_tensor(att[:], att[:], G[:, GA1, bass.ds(b, 1), :].broadcast_to([P, TB, P]), ALU.mult))
                own.link(dve.tensor_tensor(x, x, att[:], ALU.add))

            def ffn_steps(b):
                own = Chain(dve, ffn_step, 5 + 3 + FP4_STEPS + 1 + 1 + FP4_STEPS + 1 + 0, b)
                x = X[:, bass.ds(TB * b, TB), :]
                row = lambda kind: G[:, kind, bass.ds(b, 1), :].broadcast_to([P, TB, P])
                flat = lambda v: v.rearrange("p c d -> p (c d)")

                def norm_in():
                    moments(own, x, fstats, fmv, fvar)
                    dve.sem_inc(fvar_ready, 1)

                def norm_out():
                    dve.wait_ge(frstd_ready, b + 1)
                    for c in range(TB):
                        a = dve.tensor_scalar(hn[:, c, :], x[:, c, :], fmv[:, c, 0:1], frstd[:, c:c + 1], ALU.subtract, ALU.mult)
                    own.link(a)
                    own.link(dve.tensor_tensor(hn[:], hn[:], row(CB1), ALU.mult))
                    own.link(dve.tensor_tensor(hn[:], hn[:], row(SB1), ALU.add))

                todo = [(0, norm_in), (1, norm_out)]
                rounding = list(fp4_round(dve, own, flat(hn[:]), flat(hn[:]), amax[:, 0:S // QBLK], qinv[:, 0:S // QBLK],
                                          size[:, 0:S], low[:, 0:S], S))
                assert len(rounding) == FP4_STEPS
                todo += [(2 + n // 6, do) for n, do in enumerate(rounding)]
                todo.append((4, lambda: dve.sem_inc(h_ready, 1)))

                def gated(c):
                    dve.wait_ge(f_free, FJ * b + c + 3)
                    dve.wait_ge(u_full, UJ * b + c + 1)
                    own.link(dve.tensor_tensor(mid[:, c, :], gate[:, c, :], U_bank[:, 0:FI], ALU.mult))
                    dve.sem_inc(u_free, 1)
                todo += [(FFN_AT[1], lambda: gated(0)), (FFN_AT[2], lambda: gated(1))]
                rounding = list(fp4_round(dve, own, flat(mid[:]), flat(mid[:]), amax[:], qinv[:], size[:], low[:], TB * FI))
                todo += [(FFN_AT[2] + 1 + n // 3, do) for n, do in enumerate(rounding)]
                todo.append((FFN_AT[2] + 1 + (FP4_STEPS - 1) // 3, lambda: dve.sem_inc(m_ready, 1)))

                def finish():
                    dve.wait_ge(u_full, UJ * b + 3)
                    own.link(dve.tensor_tensor(fy[:], U_bank[:, 0:S].rearrange("p (c d) -> p c d", c=TB), row(GB1), ALU.mult))
                    dve.sem_inc(u_free, 1)
                todo.append((FFN_AT[5], finish))
                return todo, own

            def store(b, par, count):
                dve.wait_ge(stored[par], 16 * (count + 1))
                dve.tensor_tensor(res[:, par, :, :], X[:, bass.ds(TB * b, TB), :], fy[:], ALU.add).then_inc(res_ready, 1)

            def batch(b, par, last, first=False, half=0):
                todo, own = ffn_steps(b - 1) if not first else ([], None)
                for k in range(NSTEP):
                    if 1 <= k <= UNITS:
                        copy_turned(b, k - 1)
                    if k < UNITS:
                        row_max(b, k)
                    for at, do in todo:
                        if at == k:
                            do()
                    if not last and k == PROJECT[0] - 1:
                        prepare(b + 1, 1 - par)
                if not first:
                    store(b - 1, 1 - par, half)
                    own.end()
                attended(b, par)

            dve.sem_inc(pT_ready, 2)
            dve.sem_inc(pv_done, 2)
            dve.sem_inc(u_free, 1)
            dve.sem_inc(att_step, 5)
            dve.wait_ge(w_in, 5 * 16)
            dve.tensor_copy(index[:, 0, :, :], slot[:, :, 0:TB]).then_inc(index_ready, 1)
            prepare(0, 0)
            batch(0, 0, False, first=True)
            with dve.Fori(0, B // 2 - 1) as i:
                batch(2 * i + 1, 1, False, half=i)
                batch(2 * i + 2, 0, False, half=i)
            batch(B - 1, 1, True, half=B // 2 - 1)
            todo, own = ffn_steps(B - 1)
            for at, do in todo:
                do()
            store(B - 1, 1, B // 2 - 1)
            own.end()


def kernel(**inputs):
    import numpy as np
    import concourse.bacc as bacc
    from concourse.bass_utils import run_bass_kernel_spmd

    def transposed(name):
        a = np.asarray(inputs[name])
        return np.ascontiguousarray(np.swapaxes(a, -1, -2))

    p = np.arange(P)
    eq = lambda a, b: (a[:, None] == b[None, :]).astype(np.float32)
    query_of, head_of = p // HG, p % HG
    arrays = {
        "ident": np.eye(P, dtype=np.float32),
        "ones": np.ones((1, P), np.float32),
        "head_mask": eq(p // DH, np.arange(NH)).reshape(P, 2, HG),
        "pick": np.concatenate([eq(head_of, np.arange(HG)), eq(query_of, np.arange(QB)[::-1])], 1),
    }
    left, right = 255 - MRP, 512 - (255 + MRP + 1)
    embK, embV = np.asarray(inputs["L0_attn_embK"]), np.asarray(inputs["L0_attn_embV"])
    extend = lambda a: np.concatenate([np.repeat(a[:1], left, 0), a, np.repeat(a[-1:], right, 0)], 0)
    arrays["ek_ext"] = np.ascontiguousarray(extend(embK).T)
    arrays["rv_ext"] = extend(embV)
    arrays["x"] = np.asarray(inputs["L0_attn_x"]).reshape(B * S, P)
    for layer in range(2):
        arrays[f"c{layer}T"] = transposed(f"L{layer}_c")
        arrays[f"L{layer}_wmod"] = np.asarray(inputs[f"L{layer}_wmod"])
    for k in "qkvo":
        arrays[f"W{k}T"] = transposed(f"L0_attn_W{k}")
        arrays[f"b{k}"] = np.asarray(inputs[f"L0_attn_b{k}"])
    arrays["WqdT"] = np.ascontiguousarray(arrays["WqT"].reshape(P, NH, DH).swapaxes(1, 2).reshape(P, P))
    arrays["bqd"] = np.ascontiguousarray(arrays["bq"].reshape(NH, DH).T.reshape(1, P))
    arrays["WrT"] = transposed("L0_ffn_Wr")
    arrays["gamma"] = np.asarray(inputs["L0_ffn_ln_gamma"])
    arrays["beta"] = np.asarray(inputs["L0_ffn_ln_beta"])
    arrays["W12T"] = transposed("L0_ffn_W12")
    arrays["W3T"] = transposed("L0_ffn_W3")
    arrays["order"] = np.broadcast_to(E - np.arange(E), (P, E)).astype(np.float32)
    bf16 = mybir.dt.np(BF16)
    arrays["before"] = (p[:, None] < p[None, :]).astype(bf16)
    arrays["all_ones"] = np.ones((P, P), bf16)
    token = np.arange(NT)[None, :] * P + p[:, None]
    arrays["spare"] = np.stack([SLOTS + 2 * token, SLOTS + 2 * token + 1], 1).astype(np.float32)
    for k in ("L1_attn_Wq", "L1_attn_Wk", "L1_attn_Wv", "L1_ffn_w_gate", "L1_ffn_w_up", "L1_ffn_w_down"):
        arrays[k.replace("attn_", "").replace("L1_ffn_", "")] = np.asarray(inputs[k])
    arrays["own_head"] = eq(p // DH, np.arange(NH))
    tri = (p[:, None] <= p[None, :]).astype(np.float32)
    arrays["causal"] = np.stack([tri, tri, np.ones((P, P), np.float32)], 1)

    nc = bacc.Bacc("TRN2", target_bir_lowering=False, num_devices=1)
    t = {k: nc.dram_tensor("in_" + k, a.shape, mybir.dt.from_np(a.dtype), kind="ExternalInput").ap() for k, a in arrays.items()}
    out = nc.dram_tensor("out", (B * S, P), F32, kind="ExternalOutput").ap()
    program(nc, t, out)
    r = run_bass_kernel_spmd(nc, [{"in_" + k: a for k, a in arrays.items()}], core_ids=[0])
    return r.results[0]["out"].reshape(B, S, P)
```
